# Optimizing a Trainium2 kernel written in Bass

```python
import numpy as np
import jax
import jax.numpy as jnp

def _softmax(x, axis=-1):
    return jax.nn.softmax(x, axis=axis)

def _gelu(x):
    return jax.nn.gelu(x, approximate=True)

def _silu(x):
    return jax.nn.silu(x)

def _sigmoid(x):
    return jax.nn.sigmoid(x)

def _layernorm(x, axis=-1, eps=1e-05):
    m = jnp.mean(x, axis=axis, keepdims=True)
    v = jnp.var(x, axis=axis, keepdims=True)
    return (x - m) / jnp.sqrt(v + eps)

def _scatter_add(tgt, idx, src, axis=0):
    return tgt.at[idx].add(src)

def _segment_sum(src, seg, n):
    return jax.ops.segment_sum(src, seg, n)
kernel_name = 'mk_dlrm_tower_d1_rec_r8_b8615d'

def setup_inputs(seed: int=0):
    np.random.seed(seed)
    _w = jnp.asarray

    def _rec_inputs():
        import jax
        import jax.numpy as jnp
        _tk = jax.random.key(seed)
        ids = jnp.stack([jax.random.randint(jax.random.fold_in(_tk, 200 + f), (2048,), 0, v, jnp.int32) for f, v in enumerate([1250, 12500, 1250, 12500, 125000, 1250, 1000, 1250, 12500, 1250, 12500, 12500, 1250, 12500, 1000, 12500, 12500, 1000, 1250, 1250, 1000, 1000, 1250, 1250, 1250, 1250])], axis=1)
        tbl_0 = 0.05 * jax.random.normal(jax.random.fold_in(_tk, 500 + 0), (1250, 128), jnp.float32)
        tbl_1 = 0.05 * jax.random.normal(jax.random.fold_in(_tk, 500 + 1), (12500, 128), jnp.float32)
        tbl_2 = 0.05 * jax.random.normal(jax.random.fold_in(_tk, 500 + 2), (1250, 128), jnp.float32)
        tbl_3 = 0.05 * jax.random.normal(jax.random.fold_in(_tk, 500 + 3), (12500, 128), jnp.float32)
        tbl_4 = 0.05 * jax.random.normal(jax.random.fold_in(_tk, 500 + 4), (125000, 128), jnp.float32)
        tbl_5 = 0.05 * jax.random.normal(jax.random.fold_in(_tk, 500 + 5), (1250, 128), jnp.float32)
        tbl_6 = 0.05 * jax.random.normal(jax.random.fold_in(_tk, 500 + 6), (1000, 128), jnp.float32)
        tbl_7 = 0.05 * jax.random.normal(jax.random.fold_in(_tk, 500 + 7), (1250, 128), jnp.float32)
        tbl_8 = 0.05 * jax.random.normal(jax.random.fold_in(_tk, 500 + 8), (12500, 128), jnp.float32)
        tbl_9 = 0.05 * jax.random.normal(jax.random.fold_in(_tk, 500 + 9), (1250, 128), jnp.float32)
        tbl_10 = 0.05 * jax.random.normal(jax.random.fold_in(_tk, 500 + 10), (12500, 128), jnp.float32)
        tbl_11 = 0.05 * jax.random.normal(jax.random.fold_in(_tk, 500 + 11), (12500, 128), jnp.float32)
        tbl_12 = 0.05 * jax.random.normal(jax.random.fold_in(_tk, 500 + 12), (1250, 128), jnp.float32)
        tbl_13 = 0.05 * jax.random.normal(jax.random.fold_in(_tk, 500 + 13), (12500, 128), jnp.float32)
        tbl_14 = 0.05 * jax.random.normal(jax.random.fold_in(_tk, 500 + 14), (1000, 128), jnp.float32)
        tbl_15 = 0.05 * jax.random.normal(jax.random.fold_in(_tk, 500 + 15), (12500, 128), jnp.float32)
        tbl_16 = 0.05 * jax.random.normal(jax.random.fold_in(_tk, 500 + 16), (12500, 128), jnp.float32)
        tbl_17 = 0.05 * jax.random.normal(jax.random.fold_in(_tk, 500 + 17), (1000, 128), jnp.float32)
        tbl_18 = 0.05 * jax.random.normal(jax.random.fold_in(_tk, 500 + 18), (1250, 128), jnp.float32)
        tbl_19 = 0.05 * jax.random.normal(jax.random.fold_in(_tk, 500 + 19), (1250, 128), jnp.float32)
        tbl_20 = 0.05 * jax.random.normal(jax.random.fold_in(_tk, 500 + 20), (1000, 128), jnp.float32)
        tbl_21 = 0.05 * jax.random.normal(jax.random.fold_in(_tk, 500 + 21), (1000, 128), jnp.float32)
        tbl_22 = 0.05 * jax.random.normal(jax.random.fold_in(_tk, 500 + 22), (1250, 128), jnp.float32)
        tbl_23 = 0.05 * jax.random.normal(jax.random.fold_in(_tk, 500 + 23), (1250, 128), jnp.float32)
        tbl_24 = 0.05 * jax.random.normal(jax.random.fold_in(_tk, 500 + 24), (1250, 128), jnp.float32)
        tbl_25 = 0.05 * jax.random.normal(jax.random.fold_in(_tk, 500 + 25), (1250, 128), jnp.float32)
        _rk = jax.random.fold_in(_tk, 7)
        r_bottom_output = -0.000520686 + 1.00062 * jax.random.normal(jax.random.fold_in(_rk, 101), (2048, 128), jnp.float32)
        W_top1 = 0.0456912 * jax.random.normal(jax.random.fold_in(_tk, 801), (479, 512), jnp.float32)
        W_top2 = 0.0441942 * jax.random.normal(jax.random.fold_in(_tk, 802), (512, 256), jnp.float32)
        W_top3 = 0.0625 * jax.random.normal(jax.random.fold_in(_tk, 803), (256, 1), jnp.float32)
        b_top1 = jnp.zeros((512,), jnp.float32)
        b_top2 = jnp.zeros((256,), jnp.float32)
        return (r_bottom_output, ids, tbl_0, tbl_1, tbl_2, tbl_3, tbl_4, tbl_5, tbl_6, tbl_7, tbl_8, tbl_9, tbl_10, tbl_11, tbl_12, tbl_13, tbl_14, tbl_15, tbl_16, tbl_17, tbl_18, tbl_19, tbl_20, tbl_21, tbl_22, tbl_23, tbl_24, tbl_25, W_top1, b_top1, W_top2, b_top2, W_top3)
    r_bottom_output, ids, tbl_0, tbl_1, tbl_2, tbl_3, tbl_4, tbl_5, tbl_6, tbl_7, tbl_8, tbl_9, tbl_10, tbl_11, tbl_12, tbl_13, tbl_14, tbl_15, tbl_16, tbl_17, tbl_18, tbl_19, tbl_20, tbl_21, tbl_22, tbl_23, tbl_24, tbl_25, W_top1, b_top1, W_top2, b_top2, W_top3 = _rec_inputs()

    def _L0_rec_setup():
        import jax, jax.numpy as jnp
        import numpy as np
        NUM_FEATURES = 27
        _TRIU_I, _TRIU_J = np.triu_indices(NUM_FEATURES, k=1)
        key = jax.random.key(seed)
        k1, k2 = jax.random.split(key)
        bottom_output = jax.random.normal(k1, (2048, 128), dtype=jnp.float32)
        embeddings = jax.random.normal(k2, (2048, 26, 128), dtype=jnp.float32)
        return {'bottom_output': bottom_output, 'embeddings': embeddings}
    _L0_rec_all = _L0_rec_setup()
    _L0_rec_in = {k: v for k, v in _L0_rec_all.items() if k in ()}
    del _L0_rec_all
    return {'r_bottom_output': r_bottom_output, 'ids': ids, 'tbl_0': tbl_0, 'tbl_1': tbl_1, 'tbl_2': tbl_2, 'tbl_3': tbl_3, 'tbl_4': tbl_4, 'tbl_5': tbl_5, 'tbl_6': tbl_6, 'tbl_7': tbl_7, 'tbl_8': tbl_8, 'tbl_9': tbl_9, 'tbl_10': tbl_10, 'tbl_11': tbl_11, 'tbl_12': tbl_12, 'tbl_13': tbl_13, 'tbl_14': tbl_14, 'tbl_15': tbl_15, 'tbl_16': tbl_16, 'tbl_17': tbl_17, 'tbl_18': tbl_18, 'tbl_19': tbl_19, 'tbl_20': tbl_20, 'tbl_21': tbl_21, 'tbl_22': tbl_22, 'tbl_23': tbl_23, 'tbl_24': tbl_24, 'tbl_25': tbl_25, 'W_top1': W_top1, 'b_top1': b_top1, 'W_top2': W_top2, 'b_top2': b_top2, 'W_top3': W_top3}

def reference(r_bottom_output, ids, tbl_0, tbl_1, tbl_2, tbl_3, tbl_4, tbl_5, tbl_6, tbl_7, tbl_8, tbl_9, tbl_10, tbl_11, tbl_12, tbl_13, tbl_14, tbl_15, tbl_16, tbl_17, tbl_18, tbl_19, tbl_20, tbl_21, tbl_22, tbl_23, tbl_24, tbl_25, W_top1, b_top1, W_top2, b_top2, W_top3):
    import jax
    import jax.numpy as jnp

    def _L0_rec_ref(bottom_output, embeddings):
        import jax, jax.numpy as jnp
        import numpy as np
        NUM_FEATURES = 27
        _TRIU_I, _TRIU_J = np.triu_indices(NUM_FEATURES, k=1)
        all_emb = jnp.concatenate([bottom_output[:, None, :], embeddings], axis=1)
        gram = jnp.einsum('bfd,bgd->bfg', all_emb, all_emb)
        return gram[:, _TRIU_I, _TRIU_J]
    e = jnp.stack([tbl_0[ids[:, 0]], tbl_1[ids[:, 1]], tbl_2[ids[:, 2]], tbl_3[ids[:, 3]], tbl_4[ids[:, 4]], tbl_5[ids[:, 5]], tbl_6[ids[:, 6]], tbl_7[ids[:, 7]], tbl_8[ids[:, 8]], tbl_9[ids[:, 9]], tbl_10[ids[:, 10]], tbl_11[ids[:, 11]], tbl_12[ids[:, 12]], tbl_13[ids[:, 13]], tbl_14[ids[:, 14]], tbl_15[ids[:, 15]], tbl_16[ids[:, 16]], tbl_17[ids[:, 17]], tbl_18[ids[:, 18]], tbl_19[ids[:, 19]], tbl_20[ids[:, 20]], tbl_21[ids[:, 21]], tbl_22[ids[:, 22]], tbl_23[ids[:, 23]], tbl_24[ids[:, 24]], tbl_25[ids[:, 25]]], axis=1)
    z = _L0_rec_ref(r_bottom_output, e)
    z = z.reshape(z.shape[0], -1)
    h = jnp.concatenate([z, r_bottom_output], axis=1)
    h = jnp.maximum(h @ W_top1 + b_top1, 0.0)
    h = jnp.maximum(h @ W_top2 + b_top2, 0.0)
    y = h @ W_top3
    return y

_drawn_inputs = setup_inputs


def setup_inputs(seed=0):
    import zlib

    import numpy as np

    out = dict(_drawn_inputs(seed))
    spreads = {'b_top1': (0.0, 0.1), 'b_top2': (0.0, 0.1)}
    factors = {}
    for name, (base, spread) in spreads.items():
        noise = np.random.default_rng([zlib.crc32(name.encode()), seed]).standard_normal(out[name].shape)
        drawn = base * np.exp(spread * noise) if base else spread * noise
        out[name] = jnp.asarray(drawn.astype(out[name].dtype))
    for name, factor in factors.items():
        out[name] = (out[name] * factor).astype(out[name].dtype)
    return out
```

```python
import concourse.bass as bass
from concourse import mybir
from contextlib import ExitStack

P = 128
BATCH = 2048
TILES = BATCH // P
D = 128
TABLES = 26
SLOTS = TABLES + 1
PAD = 32
GRP = P // 4
NG = SLOTS - 1
N1, N2 = 512, 256
C1 = N1 // P
PAIRS = SLOTS * (SLOTS - 1) // 2
HALF = SLOTS // 2
CHUNKS = [min(P, PAIRS - P * c) for c in range(-(-PAIRS // P))]
ROUND = 4
ROUNDS = -(-SLOTS // ROUND)
EVEN_ROUNDS, ODD_ROUNDS = (ROUNDS + 1) // 2, ROUNDS // 2
GROUPS_PER_STEP = 8
GRAM_STEPS = GRP // GROUPS_PER_STEP


def pair_row(f, g):
    return f * SLOTS - f * (f + 1) // 2 + g - f - 1


def w1_pieces():
    runs = [(SLOTS * max(0, f - HALF) + f, SLOTS, HALF - max(0, f - HALF), pair_row(f, HALF + 1 + max(0, f - HALF)))
            for f in range(SLOTS - 1)]
    runs += [(SLOTS * r + HALF + 1 + r, 1, HALF - r, pair_row(r, r + 1)) for r in range(HALF)]
    pieces = []
    for at, pitch, count, row in runs:
        for c in range(len(CHUNKS)):
            inside = [k for k in range(count) if P * c <= at + pitch * k < P * (c + 1)]
            if inside:
                pieces.append((c, at + pitch * inside[0] - P * c, pitch, len(inside), row + inside[0]))
    return pieces


def build(nc, bottom, ids, tables, w1, b1, w2, b2, w3, out):
    fp32 = mybir.dt.float32
    ALU = mybir.AluOpType
    ACT = mybir.ActivationFunctionType

    bottom_v = bottom.rearrange("(p t) d -> p t d", t=TILES)
    ids_v = ids.rearrange("(p t) f -> p t f", t=TILES)

    with ExitStack() as ctx:
        def sb(name, shape, dt=fp32):
            return ctx.enter_context(nc.sbuf_tensor(name, shape, dt))

        def ps(name, shape):
            return ctx.enter_context(nc.psum_tensor(name, shape, fp32))

        def sem(name):
            return ctx.enter_context(nc.semaphore(name))

        ident = sb("ident", [P, P])
        idx = [sb(f"idx{s}", [P, TABLES], mybir.dt.int32) for s in range(2)]
        X = [sb(f"X{s}", [P, SLOTS, D]) for s in range(2)]
        XT = [sb(f"XT{s}", [P, P, PAD]) for s in range(2)]
        gram_sb = sb("gram_sb", [P, NG, GRP])
        Z = sb("Z", [P, NG, PAD])
        folded = sb("folded", [P, HALF, SLOTS])
        low_mask = sb("low_mask", [P, HALF, HALF])
        ZT = sb("ZT", [P, len(CHUNKS), P])
        bottomT = [sb(f"bottomT{s}", [P, P]) for s in range(2)]
        w1_sb = sb("w1_sb", [P, len(CHUNKS) + 1, N1])
        w2_sb = sb("w2_sb", [P, C1, N2])
        b1_sb = sb("b1_sb", [P, C1])
        b2_sb = sb("b2_sb", [P, N2])
        w3_sb = sb("w3_sb", [P, N2])
        h1 = sb("h1", [P, N1])
        h1T = sb("h1T", [P, C1, P])
        h2 = sb("h2", [P, N2])
        prod = sb("prod", [P, N2])
        ysum = sb("ysum", [P, 1])
        y = sb("y", [P, TILES])

        xt_ps = [ps(f"xt_ps{k}", [P, ROUND, P]) for k in range(2)]
        gram_ps = [ps(f"gram_ps{k}", [P, 2, 512]) for k in range(2)]
        t_ps = ps("t_ps", [P, C1, P])
        h_ps = ps("h_ps", [P, N1])

        ids_in = [sem(f"ids_in{s}") for s in range(2)]
        bottom_in = [sem(f"bottom_in{s}") for s in range(2)]
        gathered = [[sem(f"gathered{s}_{r}") for r in range(ROUNDS)] for s in range(2)]
        mask_ones = sem("mask_ones")
        mask_ready = sem("mask_ready")
        folded_high = sem("folded_high")
        folded_all = sem("folded_all")
        bottomt_moved = sem("bottomt_moved")
        ident_zero = sem("ident_zero")
        ident_ready = sem("ident_ready")
        pads_zero = sem("pads_zero")
        w1_in = sem("w1_in")
        w2_in = sem("w2_in")
        vecs_in = sem("vecs_in")
        xt_full = [sem(f"xt_full{k}") for k in range(2)]
        xt_moved = [sem(f"xt_moved{k}") for k in range(2)]
        gram_full = sem("gram_full")
        gram_dve = sem("gram_dve")
        gram_act = sem("gram_act")
        z_ready = sem("z_ready")
        zt_full = sem("zt_full")
        zt_moved = sem("zt_moved")
        h1_full = sem("h1_full")
        h1_moved = sem("h1_moved")
        h1t_full = sem("h1t_full")
        h1t_moved = sem("h1t_moved")
        h2_full = sem("h2_full")
        h2_moved = sem("h2_moved")
        prod_done = sem("prod_done")
        y_ready = sem("y_ready")
        y_out = sem("y_out")
        load_steps = sem("load_steps")
        gather_steps = sem("gather_steps")
        fold_steps = sem("fold_steps")

        block = ctx.enter_context(nc.Block())

        def tables_of(r):
            return [k - 1 for k in range(max(1, ROUND * r), min(SLOTS, ROUND * (r + 1)))]

        def slots_of(r):
            return min(ROUND, SLOTS - ROUND * r)

        def wait(eng, s, value):
            if not (isinstance(value, int) and value <= 0):
                eng.wait_ge(s, value)

        def pipeline(eng, step):
            step(0, 0, 0, False)
            step(1, 0, 1, True)
            with eng.Fori(1, TILES // 2) as n:
                step(2 * n, n, 0, True)
                step(2 * n + 1, n, 1, True)

        @block.sync
        def _(sp):
            def load_tile(t, s):
                wait(sp, xt_full[0], EVEN_ROUNDS * (t - 1))
                sp.sem_inc(load_steps, 1)
                sp.dma_start(idx[s][:], ids_v[:, t, :]).then_inc(ids_in[s], 16)
                sp.dma_start(X[s][:, 0, :], bottom_v[:, t, :]).then_inc(bottom_in[s], 16)

            load_tile(0, 0)
            load_tile(1, 1)
            for c, row, pitch, count, w_row in w1_pieces():
                sp.dma_start(w1_sb[row:row + pitch * (count - 1) + 1:pitch, c, :],
                             w1[w_row:w_row + count, :]).then_inc(w1_in, 16)
            sp.dma_start(w1_sb[:, len(CHUNKS), :], w1[PAIRS:PAIRS + D, :]).then_inc(w1_in, 16)
            sp.dma_start(w2_sb[:], w2.rearrange("(p c) n -> p c n", c=C1)).then_inc(w2_in, 16)
            sp.dma_start(b1_sb[:], b1.rearrange("(p c) -> p c", c=C1)).then_inc(vecs_in, 16)
            sp.dma_start(b2_sb[:], b2.rearrange("(o n) -> o n", o=1).to_broadcast([P, N2])).then_inc(vecs_in, 16)
            sp.dma_start(w3_sb[:], w3.rearrange("n o -> o n").to_broadcast([P, N2])).then_inc(vecs_in, 16)
            with sp.Fori(1, TILES // 2) as n:
                load_tile(2 * n, 0)
                load_tile(2 * n + 1, 1)
            sp.wait_ge(y_ready, TILES)
            sp.dma_start(out.rearrange("(p t) o -> p (t o)", t=TILES), y[:]).then_inc(y_out, 16)
            sp.wait_ge(y_out, 16)

        w1_loads = 1 + len(w1_pieces())

        @block.gpsimd
        def _(pool):
            def gather(t, n, s):
                pool.wait_ge(ids_in[s], 16 * (n + 1))
                wait(pool, xt_full[0], EVEN_ROUNDS * (t - 1))
                pool.sem_inc(gather_steps, 1)
                for r in range(ROUNDS):
                    for f in tables_of(r):
                        pool.indirect_dma_start(X[s][:, 1 + f, :], None, tables[f],
                                                bass.IndirectOffsetOnAxis(idx[s][:, f:f + 1], 0)
                                                ).then_inc(gathered[s][r], 16)

            pool.memset(ident[:], 0.0).then_inc(ident_zero, 1)
            pool.wait_ge(ident_zero, 1)
            pool.affine_select(out=ident[:], in_=ident[:], compare_op=ALU.not_equal, fill=1.0, base=0,
                               pattern=[[-1, P]], channel_multiplier=1).then_inc(ident_ready, 1)
            pool.memset(low_mask[:], 1.0).then_inc(mask_ones, 1)
            pool.wait_ge(mask_ones, 1)
            pool.affine_select(out=low_mask[:], in_=low_mask[:], compare_op=ALU.is_ge, fill=0.0, base=0,
                               pattern=[[-1, HALF], [1, HALF]], channel_multiplier=0).then_inc(mask_ready, 1)
            gather(0, 0, 0)
            gather(1, 0, 1)
            with pool.Fori(1, TILES // 2) as n:
                gather(2 * n, n, 0)
                gather(2 * n + 1, n, 1)

        @block.tensor
        def _(pe):
            def transposes(t, n, s, r):
                k = r % 2
                if r == 0:
                    pe.wait_ge(bottom_in[s], 16 * (n + 1))
                pe.wait_ge(gathered[s][r], 16 * len(tables_of(r)) * (n + 1))
                wait(pe, xt_moved[k], (EVEN_ROUNDS, ODD_ROUNDS)[k] * t + r // 2)
                for j in range(slots_of(r)):
                    mm = pe.transpose(xt_ps[k][:, j, :], X[s][:, ROUND * r + j, :], ident[:])
                mm.then_inc(xt_full[k], 1)

            def gram(t, s, r):
                if r == 0:
                    pe.wait_ge(xt_moved[0], EVEN_ROUNDS * (t + 1))
                    pe.wait_ge(xt_moved[1], ODD_ROUNDS * (t + 1))
                wait(pe, gram_dve, GRAM_STEPS * t + r - 1)
                wait(pe, gram_act, GRAM_STEPS * t + r - 1)
                for k in range(GROUPS_PER_STEP):
                    grp = GROUPS_PER_STEP * r + k
                    four = XT[s][:, 4 * grp:4 * (grp + 1), :]
                    mm = pe.matmul(gram_ps[r % 2][:, k // 4, (k % 4) * 4 * NG:(k % 4 + 1) * 4 * NG],
                                   four.rearrange("d q f -> d (q f)"),
                                   four[:, :, 1:SLOTS], start=True, stop=True)
                mm.then_inc(gram_full, 1)

            def z_transposes(t):
                pe.wait_ge(folded_all, t + 1)
                pairs = folded[:].rearrange("p r c -> p (r c)")
                for c, k in enumerate(CHUNKS):
                    mm = pe.transpose(t_ps[0:k, c, :], pairs[:, P * c:P * c + k], ident[:])
                mm.then_inc(zt_full, 1)

            def layer1(t, s):
                pe.wait_ge(w1_in, 16 * w1_loads)
                pe.wait_ge(bottomt_moved, t + 1)
                pe.wait_ge(zt_moved, t + 1)
                wait(pe, h2_moved, t)
                for c, k in enumerate(CHUNKS):
                    pe.matmul(h_ps[:], ZT[0:k, c, :], w1_sb[0:k, c, :], start=(c == 0), stop=False)
                pe.matmul(h_ps[:], bottomT[s][:], w1_sb[:, len(CHUNKS), :], start=False,
                          stop=True).then_inc(h1_full, 1)

            def h1_transposes(t):
                pe.wait_ge(h1_moved, t + 1)
                chunks = h1[:].rearrange("b (p c) -> b c p", c=C1)
                for c in range(C1):
                    mm = pe.transpose(t_ps[:, c, :], chunks[:, c, :], ident[:])
                mm.then_inc(h1t_full, 1)

            def layer2(t):
                pe.wait_ge(w2_in, 16)
                pe.wait_ge(h1t_moved, C1 * (t + 1))
                for c in range(C1):
                    mm = pe.matmul(h_ps[:, 0:N2], h1T[:, c, :], w2_sb[:, c, :], start=(c == 0), stop=(c == C1 - 1))
                mm.then_inc(h2_full, 1)

            def step(t, n, s, mlp):
                transposes(t, n, s, 0)
                transposes(t, n, s, 1)
                if mlp:
                    z_transposes(t - 1)
                transposes(t, n, s, 2)
                transposes(t, n, s, 3)
                if mlp:
                    layer1(t - 1, 1 - s)
                transposes(t, n, s, 4)
                transposes(t, n, s, 5)
                if mlp:
                    h1_transposes(t - 1)
                transposes(t, n, s, 6)
                gram(t, s, 0)
                if mlp:
                    layer2(t - 1)
                for r in range(1, GRAM_STEPS):
                    gram(t, s, r)

            pe.wait_ge(ident_ready, 1)
            pe.wait_ge(pads_zero, 3)
            pipeline(pe, step)
            z_transposes(TILES - 1)
            layer1(TILES - 1, 1)
            h1_transposes(TILES - 1)
            layer2(TILES - 1)

        def move_xt(eng, copy, t, n, s, r):
            k = r % 2
            eng.wait_ge(xt_full[k], (EVEN_ROUNDS, ODD_ROUNDS)[k] * t + r // 2 + 1)
            wait(eng, gram_full, GRAM_STEPS * (t - 1))
            m = slots_of(r)
            dst = XT[s][:, :, ROUND * r:ROUND * r + m].rearrange("d (grp q) f -> d f q grp", q=4)
            copy(dst, xt_ps[k][:, 0:m, :].rearrange("d f (q grp) -> d f q grp", q=4)).then_inc(xt_moved[k], 1)

        def move_gram(eng, copy, t, r, quadrants, done):
            eng.wait_ge(gram_full, GRAM_STEPS * t + r + 1)
            wait(eng, z_ready, t)
            for q in quadrants:
                rows = slice(PAD * q, PAD * (q + 1))
                src = gram_ps[r % 2][rows, :, 0:16 * NG].rearrange("p b (m n) -> p b m n", n=4 * NG)
                dst = gram_sb[rows, :, GROUPS_PER_STEP * r:GROUPS_PER_STEP * (r + 1)]
                last = copy(dst.rearrange("p g (b m) -> p b m g", b=2), src[:, :, :, NG * q:NG * (q + 1)])
            last.then_inc(done, 1)

        @block.vector
        def _(dve):
            copy = nc.vector.tensor_copy

            def z_blocks(t):
                dve.wait_ge(gram_dve, GRAM_STEPS * (t + 1))
                dve.wait_ge(gram_act, GRAM_STEPS * (t + 1))
                wait(dve, folded_all, t)
                dve.transpose(Z[:].rearrange("p g f -> p (g f)"),
                              gram_sb[:].rearrange("p g r -> p (g r)")).then_inc(z_ready, 1)
                dve.wait_ge(z_ready, t + 1)
                wait(dve, zt_full, t)
                dve.tensor_copy(folded[:], Z[:, HALF:NG, 0:SLOTS]).then_inc(folded_high, 1)
                dve.wait_ge(folded_high, t + 1)
                dve.sem_inc(fold_steps, 1)
                dve.copy_predicated(folded[:, :, HALF + 1:SLOTS], low_mask[:].bitcast(mybir.dt.int32),
                                    Z[:, 0:HALF, 0:HALF].rearrange("p g f -> p f g")).then_inc(folded_all, 1)

            def move_bottom(t, s):
                dve.wait_ge(xt_full[0], EVEN_ROUNDS * t + 1)
                wait(dve, h1_full, t - 1)
                dve.tensor_copy(bottomT[s][:], xt_ps[0][:, 0, :]).then_inc(bottomt_moved, 1)

            def move_zt(t):
                dve.wait_ge(zt_full, t + 1)
                wait(dve, h1_full, t)
                dve.tensor_copy(ZT[:], t_ps[:, 0:len(CHUNKS), :]).then_inc(zt_moved, 1)

            def layer3(t):
                dve.wait_ge(h2_full, t + 1)
                wait(dve, prod_done, t)
                dve.tensor_tensor(h2[:], h_ps[:, 0:N2], b2_sb[:], ALU.add).then_inc(h2_moved, 1)
                dve.wait_ge(h2_moved, t + 1)
                wait(dve, y_ready, t)
                dve.scalar_tensor_tensor(prod[:], h2[:], 0.0, w3_sb[:], ALU.max, ALU.mult,
                                         accum_out=ysum[:]).then_inc(prod_done, 1)
                dve.wait_ge(prod_done, t + 1)
                dve.tensor_copy(y[:, bass.ds(t, 1)], ysum[:]).then_inc(y_ready, 1)

            def step(t, n, s, mlp):
                move_bottom(t, s)
                move_xt(dve, copy, t, n, s, 0)
                if mlp:
                    move_zt(t - 1)
                move_xt(dve, copy, t, n, s, 2)
                move_xt(dve, copy, t, n, s, 4)
                move_xt(dve, copy, t, n, s, 6)
                move_gram(dve, copy, t, 0, (0, 1), gram_dve)
                if mlp:
                    layer3(t - 1)
                for r in range(1, GRAM_STEPS):
                    move_gram(dve, copy, t, r, (0, 1), gram_dve)
                z_blocks(t)

            for s in range(2):
                dve.memset(XT[s][:, :, SLOTS:PAD], 0.0).then_inc(pads_zero, 1)
            dve.memset(t_ps[:], 0.0).then_inc(pads_zero, 1)
            dve.wait_ge(mask_ready, 1)
            dve.wait_ge(vecs_in, 48)
            pipeline(dve, step)
            move_zt(TILES - 1)
            layer3(TILES - 1)

        @block.scalar
        def _(act):
            copy = nc.scalar.copy

            def move_h1(t):
                act.wait_ge(h1_full, t + 1)
                wait(act, h1t_full, t)
                act.copy(h1[:], h_ps[:]).then_inc(h1_moved, 1)

            def relu_h1(t):
                act.wait_ge(h1t_full, t + 1)
                wait(act, h2_full, t)
                for c in range(C1):
                    act.activation(h1T[:, c, :], t_ps[:, c, :], ACT.Relu,
                                   bias=b1_sb[:, c:c + 1]).then_inc(h1t_moved, 1)

            def step(t, n, s, mlp):
                move_xt(act, copy, t, n, s, 1)
                move_xt(act, copy, t, n, s, 3)
                if mlp:
                    move_h1(t - 1)
                move_xt(act, copy, t, n, s, 5)
                if mlp:
                    relu_h1(t - 1)
                for r in range(GRAM_STEPS):
                    move_gram(act, copy, t, r, (2, 3), gram_act)

            act.wait_ge(vecs_in, 48)
            pipeline(act, step)
            move_h1(TILES - 1)
            relu_h1(TILES - 1)


_INS = (["r_bottom_output", "ids"] + [f"tbl_{f}" for f in range(TABLES)]
        + ["W_top1", "b_top1", "W_top2", "b_top2", "W_top3"])


def kernel(**inputs):
    import numpy as _np
    import concourse.bacc as _bacc
    from concourse import mybir as _mybir
    from concourse.bass_utils import run_bass_kernel_spmd as _run

    nc = _bacc.Bacc("TRN2", target_bir_lowering=False, num_devices=1)
    arrays, dram = {}, {}
    for name in _INS:
        a = _np.ascontiguousarray(inputs[name])
        arrays[f"in_{name}_dram"] = a
        dram[name] = nc.dram_tensor(f"in_{name}_dram", a.shape, _mybir.dt.from_np(a.dtype),
                                    kind="ExternalInput").ap()
    out = nc.dram_tensor("out_0_dram", (BATCH, 1), _mybir.dt.float32, kind="ExternalOutput").ap()
    build(nc, dram["r_bottom_output"], dram["ids"], [dram[f"tbl_{f}"] for f in range(TABLES)],
          dram["W_top1"], dram["b_top1"], dram["W_top2"], dram["b_top2"], dram["W_top3"], out)
    r = _run(nc, [arrays], core_ids=[0])
    return r.results[0]["out_0_dram"]
```

```python
import concourse.bass as bass
from concourse import mybir
from contextlib import ExitStack

P = 128
BATCH = 2048
TILES = BATCH // P
D = 128
TABLES = 26
SLOTS = TABLES + 1
PAD = 32
GRP = P // 4
NG = SLOTS - 1
N1, N2 = 512, 256
C1 = N1 // P
PAIRS = SLOTS * (SLOTS - 1) // 2
HALF = SLOTS // 2
CHUNKS = [min(P, PAIRS - P * c) for c in range(-(-PAIRS // P))]
ROUND = 4
GROUPS_PER_STEP = 8
GRAM_STEPS = GRP // GROUPS_PER_STEP
ROWS = 3 * PAD + SLOTS
PAIR = 2 * P
PARTS = 3


def pair_row(f, g):
    return f * SLOTS - f * (f + 1) // 2 + g - f - 1


def w1_pieces():
    runs = [(NG * (HALF - r) - HALF + r, NG - r, pair_row(r, r + 1)) for r in range(HALF + 1)]
    runs += [(NG * (HALF - r) - HALF, r, pair_row(NG - r, NG - r + 1)) for r in range(1, HALF)]
    pieces = []
    for at, count, row in runs:
        while count:
            inside = min(count, P - at % P)
            pieces.append((at // P, at % P, inside, row))
            at, count, row = at + inside, count - inside, row + inside
    return pieces


def rounds_of(slots):
    runs = []
    for k in slots:
        if runs and runs[-1][-1] == k - 1 and len(runs[-1]) < ROUND:
            runs[-1].append(k)
        else:
            runs.append([k])
    rounds = []
    for run in runs:
        if rounds and sum(map(len, rounds[-1])) + len(run) <= ROUND:
            rounds[-1].append(run)
        else:
            rounds.append([run])
    return rounds


def build(nc, bottom, ids, tables, w1, b1, w2, b2, w3, out):
    fp32, bf16, fp16, i16 = mybir.dt.float32, mybir.dt.bfloat16, mybir.dt.float16, mybir.dt.int16
    ALU = mybir.AluOpType
    ACT = mybir.ActivationFunctionType

    hot_rows = min(tbl.shape[0] for tbl in tables)
    hot = [f for f in range(TABLES) if tables[f].shape[0] == hot_rows]
    HOT = len(hot)
    HC = -(-hot_rows // P)
    HP = hot_rows // HC
    assert HC * HP == hot_rows and hot_rows <= 2048
    hot_slots = rounds_of([1 + f for f in hot])
    rounds = rounds_of([k for k in range(SLOTS) if k - 1 not in hot])
    ROUNDS = len(rounds)
    COLUMNS = SLOTS - HOT
    per_bank = ((ROUNDS + 1) // 2, ROUNDS // 2)
    first_column = [sum(len(run) for rnd in rounds[:r] for run in rnd) for r in range(ROUNDS)]
    hot_buffer = [u % 2 if u < HOT - 1 or HOT % 2 == 0 else 2 for u in range(HOT)]

    bottom_v = bottom.rearrange("(p t) d -> p t d", t=TILES)
    ids_v = ids.rearrange("(p t) f -> p t f", t=TILES)

    with ExitStack() as ctx:
        def sb(name, shape, dt=fp32):
            return ctx.enter_context(nc.sbuf_tensor(name, shape, dt))

        def ps(name, shape, dt=fp32):
            return ctx.enter_context(nc.psum_tensor(name, shape, dt))

        def sem(name):
            return ctx.enter_context(nc.semaphore(name))

        ident = sb("ident", [P, P])
        ident_bf = sb("ident_bf", [P, P], bf16)
        ident_fp16 = sb("ident_fp16", [P, P], fp16)
        ids_all = sb("ids_all", [P, TILES, TABLES], mybir.dt.int32)
        ids_hot = sb("ids_hot", [P, HOT, TILES], fp16)
        ids_wide = sb("ids_wide", [P, HOT, BATCH], fp16)
        row_number = sb("row_number", [P, HC], fp16)
        row_wide = sb("row_wide", [P, HC, PAIR], fp16)
        tab_parts = sb("tab_parts", [HP, HOT, PARTS, HC * D], bf16)
        onehot = [sb(f"onehot{k}", [HP, HC, PAIR], bf16) for k in range(max(hot_buffer) + 1)]
        hotT = sb("hotT", [P, HOT, BATCH])
        tab = [hotT[0:HP, u, BATCH - HC * D:BATCH] for u in range(HOT)]
        idx = [sb(f"idx{s}", [P, TABLES], mybir.dt.int32) for s in range(2)]
        X = [sb(f"X{s}", [P, COLUMNS, D]) for s in range(2)]
        XT = [sb(f"XT{s}", [P, P, PAD]) for s in range(2)]
        gram_sb = sb("gram_sb", [P, NG, GRP])
        Z = sb("Z", [P, NG, PAD])
        folded = sb("folded", [P, HALF + 1, NG])
        fill_mask = sb("fill_mask", [P, HALF - 1, HALF - 1])
        ZT = sb("ZT", [P, len(CHUNKS), P])
        bottomT = [sb(f"bottomT{s}", [P, P]) for s in range(2)]
        XT16 = [x[:].rearrange("d p f -> d (p f)").bitcast(i16).rearrange("d (p c) -> d p c", p=P) for x in XT]
        w1_sb = sb("w1_sb", [P, len(CHUNKS) + 1, N1])
        w2_sb = sb("w2_sb", [P, C1, N2])
        b1_sb = sb("b1_sb", [P, C1])
        b2_sb = sb("b2_sb", [P, N2])
        w3_sb = sb("w3_sb", [P, N2])
        h1 = sb("h1", [P, N1])
        h1T = sb("h1T", [P, C1, P])
        h2 = sb("h2", [P, N2])
        prod = sb("prod", [P, N2])
        ysum = sb("ysum", [P, 1])
        y = sb("y", [P, TILES])

        xt_ps = [ps(f"xt_ps{k}", [P, 2 * ROUND, P], bf16) for k in range(2)]
        gram_ps = ps("gram_ps", [P, 2, 512])
        hot_ps = ps("hot_ps", [P, PAIR])
        t_ps = ps("t_ps", [P, C1, P])
        h_ps = ps("h_ps", [P, N1])

        ids_in = [sem(f"ids_in{s}") for s in range(2)]
        bottom_in = [sem(f"bottom_in{s}") for s in range(2)]
        gathered = [[sem(f"gathered{s}_{r}") for r in range(ROUNDS)] for s in range(2)]
        mask_ones = sem("mask_ones")
        mask_ready = sem("mask_ready")
        folded_high = sem("folded_high")
        folded_all = sem("folded_all")
        bottomt_moved = sem("bottomt_moved")
        ident_zero = sem("ident_zero")
        ident_ready = sem("ident_ready")
        pads_zero = sem("pads_zero")
        w1_in = sem("w1_in")
        w2_in = sem("w2_in")
        vecs_in = sem("vecs_in")
        xt_full = [sem(f"xt_full{k}") for k in range(2)]
        xt_moved = [sem(f"xt_moved{k}") for k in range(2)]
        gram_full = sem("gram_full")
        gram_dve = sem("gram_dve")
        gram_act = sem("gram_act")
        z_ready = sem("z_ready")
        zt_full = sem("zt_full")
        zt_moved = sem("zt_moved")
        h1_full = sem("h1_full")
        h1_moved = sem("h1_moved")
        h1t_full = sem("h1t_full")
        h1t_moved = sem("h1t_moved")
        h2_full = sem("h2_full")
        h2_moved = sem("h2_moved")
        prod_done = sem("prod_done")
        y_ready = sem("y_ready")
        y_out = sem("y_out")
        all_ids_in = sem("all_ids_in")
        ids_hot_ready = sem("ids_hot_ready")
        idents_cast = sem("idents_cast")
        rows_counted = sem("rows_counted")
        rows_wide = sem("rows_wide")
        tab_in = [sem(f"tab_in{u}") for u in range(HOT)]
        tab_cast = [sem(f"tab_cast{k}") for k in range(2)]
        tab_rest = sem("tab_rest")
        tab_last = sem("tab_last")
        wide_full = sem("wide_full")
        wide_moved = sem("wide_moved")
        onehot_ready = sem("onehot_ready")
        hot_full = sem("hot_full")
        hot_moved = sem("hot_moved")
        hot_steps = sem("hot_steps")
        hot_placed = sem("hot_placed")
        load_steps = sem("load_steps")
        gather_steps = sem("gather_steps")
        fold_steps = sem("fold_steps")

        block = ctx.enter_context(nc.Block())

        def slots_of(r):
            return [k for run in rounds[r] for k in run]

        def tables_of(r):
            return [k - 1 for k in slots_of(r) if k > 0]

        moves = [sum(len(rounds[r]) for r in range(k, ROUNDS, 2)) for k in range(2)]

        hot_moves, u0 = [], 0
        for rnd in hot_slots:
            for run in rnd:
                hot_moves.append((u0, run))
                u0 += len(run)

        def moves_before(r):
            return sum(len(rounds[q]) for q in range(r % 2, r, 2))

        def wait(eng, s, value):
            if not (isinstance(value, int) and value <= 0):
                eng.wait_ge(s, value)

        def pipeline(eng, step):
            last = TILES // 2 - 1
            step(0, 0, 0, False, True)
            step(1, 0, 1, True, True)
            with eng.Fori(1, last) as n:
                step(2 * n, n, 0, True, True)
                step(2 * n + 1, n, 1, True, True)
            step(2 * last, last, 0, True, False)
            step(2 * last + 1, last, 1, True, False)

        SPREADS = HOT * TILES // 4
        spread_banks = [gram_ps[:, 0, :], gram_ps[:, 1, :], t_ps[:].rearrange("p c n -> p (c n)"), h_ps[:]]

        def spreads(u):
            return HOT + u * (SPREADS - HOT) // HOT

        def late_lookup(t, s):
            return s == 0 and not (isinstance(t, int) and t == 0)

        @block.sync
        def _(sp):
            def load_tile(t, s):
                wait(sp, xt_full[1], per_bank[1] * (t - 1))
                sp.sem_inc(load_steps, 1)
                sp.dma_start(idx[s][:], ids_v[:, t, :]).then_inc(ids_in[s], 16)
                sp.dma_start(X[s][:, 0, :], bottom_v[:, t, :]).then_inc(bottom_in[s], 16)

            load_tile(0, 0)
            sp.dma_start(ids_all[:], ids_v).then_inc(all_ids_in, 16)
            for u, f in enumerate(hot):
                sp.dma_start(tab[u], tables[f].rearrange("(p c) d -> p (c d)", p=HP)).then_inc(tab_in[u], 16)
            load_tile(1, 1)
            for c, row, count, w_row in w1_pieces():
                sp.dma_start(w1_sb[row:row + count, c, :], w1[w_row:w_row + count, :]).then_inc(w1_in, 16)
            sp.dma_start(w1_sb[:, len(CHUNKS), :], w1[PAIRS:PAIRS + D, :]).then_inc(w1_in, 16)
            sp.dma_start(w2_sb[:], w2.rearrange("(p c) n -> p c n", c=C1)).then_inc(w2_in, 16)
            sp.dma_start(b1_sb[:], b1.rearrange("(p c) -> p c", c=C1)).then_inc(vecs_in, 16)
            sp.dma_start(b2_sb[:], b2.rearrange("(o n) -> o n", o=1).to_broadcast([P, N2])).then_inc(vecs_in, 16)
            sp.dma_start(w3_sb[:], w3.rearrange("n o -> o n").to_broadcast([P, N2])).then_inc(vecs_in, 16)
            with sp.Fori(1, TILES // 2) as n:
                load_tile(2 * n, 0)
                load_tile(2 * n + 1, 1)
            sp.wait_ge(y_ready, TILES)
            sp.dma_start(out.rearrange("(p t) o -> p (t o)", t=TILES), y[:]).then_inc(y_out, 16)
            sp.wait_ge(y_out, 16)

        w1_loads = 1 + len(w1_pieces())

        @block.gpsimd
        def _(pool):
            def gather(t, n, s):
                pool.wait_ge(ids_in[s], 16 * (n + 1))
                wait(pool, xt_full[1], per_bank[1] * (t - 1))
                pool.sem_inc(gather_steps, 1)
                for r in range(ROUNDS):
                    for f in tables_of(r):
                        column = first_column[r] + slots_of(r).index(1 + f)
                        pool.indirect_dma_start(X[s][:, column, :], None, tables[f],
                                                bass.IndirectOffsetOnAxis(idx[s][:, f:f + 1], 0)
                                                ).then_inc(gathered[s][r], 16)

            pool.memset(ident[:], 0.0).then_inc(ident_zero, 1)
            pool.wait_ge(ident_zero, 1)
            pool.affine_select(out=ident[:], in_=ident[:], compare_op=ALU.not_equal, fill=1.0, base=0,
                               pattern=[[-1, P]], channel_multiplier=1).then_inc(ident_ready, 1)
            pool.memset(fill_mask[:], 1.0).then_inc(mask_ones, 1)
            pool.wait_ge(mask_ones, 1)
            pool.affine_select(out=fill_mask[:], in_=fill_mask[:], compare_op=ALU.is_ge, fill=0.0,
                               base=HALF - 2, pattern=[[-1, HALF - 1], [-1, HALF - 1]], channel_multiplier=0).then_inc(mask_ready, 1)
            pool.iota(row_number[:], pattern=[[1, HC]], base=0, channel_multiplier=HC,
                      allow_small_or_imprecise_dtypes=True).then_inc(rows_counted, 1)
            gather(0, 0, 0)
            gather(1, 0, 1)
            with pool.Fori(1, TILES // 2) as n:
                gather(2 * n, n, 0)
                gather(2 * n + 1, n, 1)

        @block.tensor
        def _(pe):
            def spread_ids(k_from, k_to):
                for k in range(k_from, k_to):
                    u, four = k % HOT, k // HOT
                    wait(pe, wide_moved, k - 3)
                    for j in range(4):
                        t = 4 * four + j
                        mm = pe.matmul(spread_banks[k % 4][:, P * j:P * (j + 1)],
                                       ids_hot[:, u, t:t + 1].to_broadcast([P, P]), ident_fp16[:],
                                       start=True, stop=True)
                    mm.then_inc(wide_full, 1)

            def lookup(m, u, part_from, part_to):
                if part_from == 0:
                    pe.wait_ge(onehot_ready, HOT * m + u + 1)
                    wait(pe, hot_moved, HOT * m + u)
                for k in range(part_from, part_to):
                    part, c = k // HC, k % HC
                    mm = pe.matmul(hot_ps[:], tab_parts[:, u, part, D * c:D * (c + 1)],
                                   onehot[hot_buffer[u]][:, c, :], start=(k == 0), stop=(k == PARTS * HC - 1))
                if part_to == PARTS * HC:
                    mm.then_inc(hot_full, 1)

            def lookup_segment(m, j):
                half = PARTS * HC // 2
                lookup(m, j // 2, half * (j % 2), half * (j % 2 + 1))

            def transposes(t, n, s, r):
                k = r % 2
                if r == 0:
                    pe.wait_ge(bottom_in[s], 16 * (n + 1))
                pe.wait_ge(gathered[s][r], 16 * len(tables_of(r)) * (n + 1))
                wait(pe, xt_moved[k], moves[k] * t + moves_before(r))
                for j in range(len(slots_of(r))):
                    halves = X[s][:, first_column[r] + j, :].bitcast(bf16).rearrange("p (d h) -> p h d", h=2)
                    for h in range(2):
                        mm = pe.transpose(xt_ps[k][:, 2 * j + h, :], halves[:, h, :], ident_bf[:])
                mm.then_inc(xt_full[k], 1)

            def gram(t, s, r):
                if r == 0:
                    pe.wait_ge(xt_moved[0], moves[0] * (t + 1))
                    pe.wait_ge(xt_moved[1], moves[1] * (t + 1))
                    pe.wait_ge(hot_placed, len(hot_moves) * (t + 1))
                wait(pe, gram_dve, GRAM_STEPS * t + r)
                wait(pe, gram_act, GRAM_STEPS * t + r)
                for k in range(GROUPS_PER_STEP):
                    grp = GROUPS_PER_STEP * r + k
                    four = XT[s][:, 4 * grp:4 * (grp + 1), :]
                    mm = pe.matmul(gram_ps[0:ROWS, k // 4, (k % 4) * 4 * NG:(k % 4 + 1) * 4 * NG],
                                   four.rearrange("d q f -> d (q f)")[:, 0:ROWS], four[:, :, 1:SLOTS],
                                   start=True, stop=True)
                mm.then_inc(gram_full, 1)

            def z_transposes(t):
                pe.wait_ge(folded_all, t + 1)
                pairs = folded[:].rearrange("p r c -> p (r c)")[:, HALF:HALF + PAIRS]
                for c, k in enumerate(CHUNKS):
                    mm = pe.transpose(t_ps[0:k, c, :], pairs[:, P * c:P * c + k], ident[:])
                mm.then_inc(zt_full, 1)

            def layer1(t, s):
                pe.wait_ge(w1_in, 16 * w1_loads)
                pe.wait_ge(bottomt_moved, t + 1)
                pe.wait_ge(zt_moved, t + 1)
                wait(pe, h2_moved, t)
                for c, k in enumerate(CHUNKS):
                    pe.matmul(h_ps[:], ZT[0:k, c, :], w1_sb[0:k, c, :], start=(c == 0), stop=False)
                pe.matmul(h_ps[:], bottomT[s][:], w1_sb[:, len(CHUNKS), :], start=False,
                          stop=True).then_inc(h1_full, 1)

            def h1_transposes(t):
                pe.wait_ge(h1_moved, t + 1)
                chunks = h1[:].rearrange("b (p c) -> b c p", c=C1)
                for c in range(C1):
                    mm = pe.transpose(t_ps[:, c, :], chunks[:, c, :], ident[:])
                mm.then_inc(h1t_full, 1)

            def layer2(t):
                pe.wait_ge(w2_in, 16)
                pe.wait_ge(h1t_moved, C1 * (t + 1))
                for c in range(C1):
                    mm = pe.matmul(h_ps[:, 0:N2], h1T[:, c, :], w2_sb[:, c, :], start=(c == 0), stop=(c == C1 - 1))
                mm.then_inc(h2_full, 1)

            def step(t, n, s, mlp, lookups):
                segments = iter(range(4) if s == 0 else range(4, 2 * HOT - 1))

                def segment():
                    if lookups:
                        lookup_segment(n + 1, next(segments))

                transposes(t, n, s, 0)
                transposes(t, n, s, 1)
                if late_lookup(t, s):
                    lookup_segment(n, 2 * HOT - 1)
                if s == 1:
                    segment()
                transposes(t, n, s, 2)
                transposes(t, n, s, 3)
                if mlp:
                    z_transposes(t - 1)
                transposes(t, n, s, 4)
                transposes(t, n, s, 5)
                if mlp:
                    layer1(t - 1, 1 - s)
                segment()
                if mlp:
                    h1_transposes(t - 1)
                gram(t, s, 0)
                if mlp:
                    layer2(t - 1)
                gram(t, s, 1)
                segment()
                gram(t, s, 2)
                segment()
                gram(t, s, 3)
                segment()

            assert ROUNDS == 6 and GRAM_STEPS == 4 and HOT == 5
            pe.wait_ge(idents_cast, 2)
            pe.wait_ge(ids_hot_ready, HOT)
            pe.wait_ge(pads_zero, 3)
            spread_ids(0, HOT)
            for u in range(HOT):
                pe.wait_ge(tab_cast[0], u + 1)
                pe.wait_ge(tab_cast[1], u + 1)
                pe.wait_ge(tab_last, u + 1)
                lookup(0, u, 0, PARTS * HC)
                spread_ids(spreads(u), spreads(u + 1))
            pe.wait_ge(ident_ready, 1)
            pe.wait_ge(wide_moved, SPREADS)
            pipeline(pe, step)
            z_transposes(TILES - 1)
            layer1(TILES - 1, 1)
            h1_transposes(TILES - 1)
            layer2(TILES - 1)

        def move_xt(eng, copy, t, n, s, r):
            k = r % 2
            eng.wait_ge(xt_full[k], per_bank[k] * t + r // 2 + 1)
            wait(eng, gram_full, GRAM_STEPS * (t - 1))
            j = 0
            for run in rounds[r]:
                m = len(run)
                dst = XT16[s][:, :, 2 * run[0]:2 * (run[0] + m)].rearrange("d (grp q) c -> d c q grp", q=4)
                src = xt_ps[k][:, 2 * j:2 * (j + m), :].bitcast(i16).rearrange("d c (q grp) -> d c q grp", q=4)
                copy(dst, src).then_inc(xt_moved[k], 1)
                j += m

        def move_gram(eng, copy, t, r, quadrants, done):
            eng.wait_ge(gram_full, GRAM_STEPS * t + r + 1)
            wait(eng, z_ready, t)
            for q in quadrants:
                rows = slice(PAD * q, PAD * (q + 1))
                src = gram_ps[rows, :, 0:16 * NG].rearrange("p b (m n) -> p b m n", n=4 * NG)
                dst = gram_sb[rows, :, GROUPS_PER_STEP * r:GROUPS_PER_STEP * (r + 1)]
                last = copy(dst.rearrange("p g (b m) -> p b m g", b=2), src[:, :, :, NG * q:NG * (q + 1)])
            last.then_inc(done, 1)

        @block.vector
        def _(dve):
            copy = nc.vector.tensor_copy

            def z_blocks(t):
                dve.wait_ge(gram_dve, GRAM_STEPS * (t + 1))
                dve.wait_ge(gram_act, GRAM_STEPS * (t + 1))
                wait(dve, folded_all, t)
                dve.transpose(Z[:].rearrange("p g f -> p (g f)"),
                              gram_sb[:].rearrange("p g r -> p (g r)")).then_inc(z_ready, 1)
                dve.wait_ge(z_ready, t + 1)
                wait(dve, zt_full, t)
                dve.tensor_copy(folded[:], Z[:, :, HALF::-1].rearrange("p g f -> p f g")).then_inc(folded_high, 1)
                dve.wait_ge(folded_high, t + 1)
                dve.sem_inc(fold_steps, 1)
                first = PAD * (HALF - 1) + HALF + 1 + PAD + 1
                low = Z[:].rearrange("p g f -> p (g f)")[:, first:first + (PAD + 1) * (HALF - 1)]
                dve.copy_predicated(folded[:, 1:HALF, 0:HALF - 1], fill_mask[:].bitcast(mybir.dt.int32),
                                    low.rearrange("p (r c) -> p r c", c=PAD + 1)[:, :, 0:HALF - 1]
                                    ).then_inc(folded_all, 1)

            def one_hot(m, u):
                wait(dve, wide_moved, u + 1 if isinstance(m, int) and m == 0 else SPREADS)
                before = [v for v in range(u) if hot_buffer[v] == hot_buffer[u]]
                if before:
                    dve.wait_ge(hot_full, HOT * m + before[-1] + 1)
                else:
                    last = max(v for v in range(HOT) if hot_buffer[v] == hot_buffer[u])
                    wait(dve, hot_full, HOT * (m - 1) + last + 1)
                ids_of = ids_wide[0:HP, u:u + 1, bass.ds(PAIR * m, PAIR)]
                dve.tensor_tensor(onehot[hot_buffer[u]][:], ids_of.to_broadcast([HP, HC, PAIR]),
                                  row_wide[0:HP], ALU.is_equal).then_inc(onehot_ready, 1)

            def move_zt(t):
                dve.wait_ge(zt_full, t + 1)
                wait(dve, h1_full, t)
                dve.tensor_copy(ZT[:], t_ps[:, 0:len(CHUNKS), :]).then_inc(zt_moved, 1)

            def layer3(t):
                dve.wait_ge(h2_full, t + 1)
                wait(dve, prod_done, t)
                dve.tensor_tensor(h2[:], h_ps[:, 0:N2], b2_sb[:], ALU.add).then_inc(h2_moved, 1)
                dve.wait_ge(h2_moved, t + 1)
                wait(dve, y_ready, t)
                dve.scalar_tensor_tensor(prod[:], h2[:], 0.0, w3_sb[:], ALU.max, ALU.mult,
                                         accum_out=ysum[:]).then_inc(prod_done, 1)
                dve.wait_ge(prod_done, t + 1)
                dve.tensor_copy(y[:, bass.ds(t, 1)], ysum[:]).then_inc(y_ready, 1)

            def step(t, n, s, mlp, lookups):
                if lookups and s == 0:
                    one_hot(n + 1, 0)
                move_xt(dve, copy, t, n, s, 2)
                if mlp:
                    move_zt(t - 1)
                move_xt(dve, copy, t, n, s, 4)
                if lookups:
                    one_hot(n + 1, (1, 3)[s])
                move_gram(dve, copy, t, 0, (0, 1), gram_dve)
                if mlp:
                    layer3(t - 1)
                move_gram(dve, copy, t, 1, (0, 1), gram_dve)
                if lookups and s == 1:
                    one_hot(n + 1, 4)
                move_gram(dve, copy, t, 2, (0, 1), gram_dve)
                if lookups and s == 0:
                    one_hot(n + 1, 2)
                move_gram(dve, copy, t, 3, (0, 1), gram_dve)
                z_blocks(t)

            for s in range(2):
                dve.memset(XT[s][:, :, SLOTS:PAD], 0.0).then_inc(pads_zero, 1)
            dve.memset(t_ps[:], 0.0).then_inc(pads_zero, 1)
            dve.wait_ge(ident_ready, 1)
            dve.tensor_copy(ident_fp16[:], ident[:]).then_inc(idents_cast, 1)
            dve.tensor_copy(ident_bf[:], ident[:]).then_inc(idents_cast, 1)
            dve.wait_ge(all_ids_in, 16)
            for u, f in enumerate(hot):
                dve.tensor_copy(ids_hot[:, u, :], ids_all[:, :, f]).then_inc(ids_hot_ready, 1)
            dve.wait_ge(rows_counted, 1)
            dve.tensor_copy(row_wide[:], row_number[:].rearrange("p (c o) -> p c o", o=1
                                                                 ).to_broadcast([P, HC, PAIR])).then_inc(rows_wide, 1)
            dve.wait_ge(rows_wide, 1)
            def after_part0(u):
                dve.wait_ge(tab_cast[0], u + 1)
                dve.tensor_tensor(tab[u], tab[u], tab_parts[:, u, 0, :], ALU.subtract).then_inc(tab_rest, 1)

            after_part0(0)
            for u in range(HOT):
                if u + 1 < HOT:
                    after_part0(u + 1)
                dve.wait_ge(tab_cast[1], u + 1)
                dve.tensor_tensor(tab_parts[:, u, 2, :], tab[u], tab_parts[:, u, 1, :],
                                  ALU.subtract).then_inc(tab_last, 1)
                one_hot(0, u)
            dve.wait_ge(mask_ready, 1)
            dve.wait_ge(vecs_in, 48)
            pipeline(dve, step)
            move_zt(TILES - 1)
            layer3(TILES - 1)

        @block.scalar
        def _(act):
            copy = nc.scalar.copy

            def move_bottom(t, s):
                act.wait_ge(xt_moved[0], moves[0] * t + 1)
                wait(act, h1_full, t - 1)
                act.copy(bottomT[s][:].rearrange("d (q grp) -> d q grp", q=4),
                         XT[s][:, :, 0].rearrange("d (grp q) -> d q grp", q=4)).then_inc(bottomt_moved, 1)

            def move_h1(t):
                act.wait_ge(h1_full, t + 1)
                wait(act, h1t_full, t)
                act.copy(h1[:], h_ps[:]).then_inc(h1_moved, 1)

            def relu_h1(t):
                act.wait_ge(h1t_full, t + 1)
                wait(act, h2_full, t)
                for c in range(C1):
                    act.activation(h1T[:, c, :], t_ps[:, c, :], ACT.Relu,
                                   bias=b1_sb[:, c:c + 1]).then_inc(h1t_moved, 1)

            def keep_hot(m, u):
                act.wait_ge(hot_full, HOT * m + u + 1)
                act.sem_inc(hot_steps, 1)
                act.copy(hotT[:, u, bass.ds(PAIR * m, PAIR)], hot_ps[:]).then_inc(hot_moved, 1)

            def place_hot(t, n, s):
                act.wait_ge(hot_moved, HOT * (n + 1))
                wait(act, gram_full, GRAM_STEPS * (t - 1))
                act.sem_inc(hot_steps, 1)
                for u0, run in hot_moves:
                    dst = XT[s][:, :, run[0]:run[0] + len(run)].rearrange("d (grp q) c -> d c q grp", q=4)
                    src = hotT[:, u0:u0 + len(run), bass.ds(P * t, P)].rearrange("d c (q grp) -> d c q grp", q=4)
                    act.copy(dst, src).then_inc(hot_placed, 1)

            def step(t, n, s, mlp, lookups):
                move_xt(act, copy, t, n, s, 0)
                move_xt(act, copy, t, n, s, 1)
                if late_lookup(t, s):
                    keep_hot(n, HOT - 1)
                move_xt(act, copy, t, n, s, 3)
                place_hot(t, n, s)
                move_xt(act, copy, t, n, s, 5)
                move_bottom(t, s)
                if mlp:
                    move_h1(t - 1)
                if lookups and s == 1:
                    keep_hot(n + 1, 2)
                if mlp:
                    relu_h1(t - 1)
                move_gram(act, copy, t, 0, (2, 3), gram_act)
                move_gram(act, copy, t, 1, (2, 3), gram_act)
                if lookups and s == 0:
                    keep_hot(n + 1, 0)
                move_gram(act, copy, t, 2, (2, 3), gram_act)
                if lookups and s == 1:
                    keep_hot(n + 1, 3)
                move_gram(act, copy, t, 3, (2, 3), gram_act)
                if lookups and s == 0:
                    keep_hot(n + 1, 1)

            def part0(u):
                act.wait_ge(tab_in[u], 16)
                act.copy(tab_parts[:, u, 0, :], tab[u]).then_inc(tab_cast[0], 1)

            def keep_spread(k):
                act.wait_ge(wide_full, k + 1)
                u, four = k % HOT, k // HOT
                act.copy(ids_wide[:, u, 4 * P * four:4 * P * (four + 1)], spread_banks[k % 4]
                         ).then_inc(wide_moved, 1)

            part0(0)
            part0(1)
            keep_spread(0)
            for u in range(HOT):
                act.wait_ge(tab_rest, u + 1)
                act.copy(tab_parts[:, u, 1, :], tab[u]).then_inc(tab_cast[1], 1)
                if u + 2 < HOT:
                    part0(u + 2)
                if u + 1 < HOT:
                    keep_spread(u + 1)
            for u in range(HOT):
                keep_hot(0, u)
                for k in range(spreads(u), spreads(u + 1)):
                    keep_spread(k)
            act.wait_ge(vecs_in, 48)
            pipeline(act, step)
            move_h1(TILES - 1)
            relu_h1(TILES - 1)


_INS = (["r_bottom_output", "ids"] + [f"tbl_{f}" for f in range(TABLES)]
        + ["W_top1", "b_top1", "W_top2", "b_top2", "W_top3"])


def kernel(**inputs):
    import numpy as _np
    import concourse.bacc as _bacc
    from concourse import mybir as _mybir
    from concourse.bass_utils import run_bass_kernel_spmd as _run

    nc = _bacc.Bacc("TRN2", target_bir_lowering=False, num_devices=1)
    arrays, dram = {}, {}
    for name in _INS:
        a = _np.ascontiguousarray(inputs[name])
        arrays[f"in_{name}_dram"] = a
        dram[name] = nc.dram_tensor(f"in_{name}_dram", a.shape, _mybir.dt.from_np(a.dtype),
                                    kind="ExternalInput").ap()
    out = nc.dram_tensor("out_0_dram", (BATCH, 1), _mybir.dt.float32, kind="ExternalOutput").ap()
    build(nc, dram["r_bottom_output"], dram["ids"], [dram[f"tbl_{f}"] for f in range(TABLES)],
          dram["W_top1"], dram["b_top1"], dram["W_top2"], dram["b_top2"], dram["W_top3"], out)
    r = _run(nc, [arrays], core_ids=[0])
    return r.results[0]["out_0_dram"]
```

```python
import concourse.bass as bass
from concourse import mybir
from contextlib import ExitStack

P = 128
BATCH = 2048
TILES = BATCH // P
D = 128
TABLES = 26
SLOTS = TABLES + 1
PAD = 32
GRP = P // 4
NG = SLOTS - 1
N1, N2 = 512, 256
C1 = N1 // P
PAIRS = SLOTS * (SLOTS - 1) // 2
HALF = SLOTS // 2
CHUNKS = [min(P, PAIRS - P * c) for c in range(-(-PAIRS // P))]
ROUND = 4
GROUPS_PER_STEP = 8
GRAM_STEPS = GRP // GROUPS_PER_STEP
ROWS = 3 * PAD + SLOTS
PAIR = 2 * P
PARTS = 3


def pair_row(f, g):
    return f * SLOTS - f * (f + 1) // 2 + g - f - 1


def w1_pieces():
    runs = [(NG * (HALF - r) - HALF + r, NG - r, pair_row(r, r + 1)) for r in range(HALF + 1)]
    runs += [(NG * (HALF - r) - HALF, r, pair_row(NG - r, NG - r + 1)) for r in range(1, HALF)]
    pieces = []
    for at, count, row in runs:
        while count:
            inside = min(count, P - at % P)
            pieces.append((at // P, at % P, inside, row))
            at, count, row = at + inside, count - inside, row + inside
    return pieces


def rounds_of(slots):
    rounds = []
    for first in range(0, len(slots), ROUND):
        runs = []
        for k in slots[first:first + ROUND]:
            if runs and runs[-1][-1] == k - 1:
                runs[-1].append(k)
            else:
                runs.append([k])
        rounds.append(runs)
    return rounds


def build(nc, bottom, ids, tables, w1, b1, w2, b2, w3, out):
    fp32, bf16, fp16, i16 = mybir.dt.float32, mybir.dt.bfloat16, mybir.dt.float16, mybir.dt.int16
    ALU = mybir.AluOpType
    ACT = mybir.ActivationFunctionType

    hot_rows = min(tbl.shape[0] for tbl in tables)
    hot = [f for f in range(TABLES) if tables[f].shape[0] == hot_rows]
    HOT = len(hot)
    HC = -(-hot_rows // P)
    HP = hot_rows // HC
    assert HC * HP == hot_rows and hot_rows <= 2048
    hot_slots = rounds_of([1 + f for f in hot])
    rounds = rounds_of([k for k in range(SLOTS) if k - 1 not in hot])
    ROUNDS = len(rounds)
    COLUMNS = SLOTS - HOT
    per_bank = ((ROUNDS + 1) // 2, ROUNDS // 2)
    first_column = [sum(len(run) for rnd in rounds[:r] for run in rnd) for r in range(ROUNDS)]
    hot_buffer = [u % 2 if u < HOT - 1 or HOT % 2 == 0 else 2 for u in range(HOT)]
    hot_buffers = max(hot_buffer) + 1
    first_buffer = [u % hot_buffers for u in range(HOT)]

    bottom_v = bottom.rearrange("(p t) d -> p t d", t=TILES)
    ids_v = ids.rearrange("(p t) f -> p t f", t=TILES)

    with ExitStack() as ctx:
        def sb(name, shape, dt=fp32):
            return ctx.enter_context(nc.sbuf_tensor(name, shape, dt))

        def ps(name, shape, dt=fp32):
            return ctx.enter_context(nc.psum_tensor(name, shape, dt))

        def sem(name):
            return ctx.enter_context(nc.semaphore(name))

        ident = sb("ident", [P, P])
        ident_bf = sb("ident_bf", [P, P], bf16)
        ident_fp16 = sb("ident_fp16", [P, P], fp16)
        ids_all = sb("ids_all", [P, TILES, TABLES], mybir.dt.int32)
        ids_hot = sb("ids_hot", [P, HOT, TILES], fp16)
        ids_wide = sb("ids_wide", [P, HOT, BATCH], fp16)
        row_number = sb("row_number", [P, HC], fp16)
        row_wide = sb("row_wide", [P, HC, PAIR], fp16)
        tab_parts = sb("tab_parts", [HP, HOT, PARTS, HC * D], bf16)
        onehot = [sb(f"onehot{k}", [HP, HC, PAIR], bf16) for k in range(hot_buffers)]
        hotT = sb("hotT", [P, HOT, BATCH])
        tab = [hotT[0:HP, u, BATCH - HC * D:BATCH] for u in range(HOT)]
        idx = [sb(f"idx{s}", [P, TABLES], mybir.dt.int32) for s in range(2)]
        X = [sb(f"X{s}", [P, COLUMNS, D]) for s in range(2)]
        XT = [sb(f"XT{s}", [P, P, PAD]) for s in range(2)]
        gram_sb = sb("gram_sb", [P, NG, GRP])
        Z = sb("Z", [P, NG, PAD])
        folded = sb("folded", [P, HALF + 1, NG])
        fill_mask = sb("fill_mask", [P, HALF - 1, HALF - 1])
        ZT = sb("ZT", [P, len(CHUNKS), P])
        bottomT = [sb(f"bottomT{s}", [P, P]) for s in range(2)]
        XT16 = [x[:].rearrange("d p f -> d (p f)").bitcast(i16).rearrange("d (p c) -> d p c", p=P) for x in XT]
        w1_sb = sb("w1_sb", [P, len(CHUNKS) + 1, N1])
        w2_sb = sb("w2_sb", [P, C1, N2])
        b1_sb = sb("b1_sb", [P, C1])
        b2_sb = sb("b2_sb", [P, N2])
        w3_sb = sb("w3_sb", [P, N2])
        h1T = sb("h1T", [P, C1, P])
        h2 = sb("h2", [P, N2])
        prod = sb("prod", [P, N2])
        ysum = sb("ysum", [P, 1])
        y = sb("y", [P, TILES])

        xt_ps = [ps(f"xt_ps{k}", [P, 2 * ROUND, P], bf16) for k in range(2)]
        gram_ps = ps("gram_ps", [P, 2, 512])
        hot_ps = ps("hot_ps", [P, PAIR])
        zt_ps = ps("zt_ps", [P, len(CHUNKS), P])
        h2_ps = zt_ps[:, 0:2, :].rearrange("p c n -> p (c n)")
        h1_ps = [ps(f"h1_ps{k}", [P, 512]) for k in range(2)]

        ids_in = [sem(f"ids_in{s}") for s in range(2)]
        bottom_in = [sem(f"bottom_in{s}") for s in range(2)]
        gathered = [[sem(f"gathered{s}_{r}") for r in range(ROUNDS)] for s in range(2)]
        mask_ones = sem("mask_ones")
        mask_ready = sem("mask_ready")
        folded_high = sem("folded_high")
        folded_all = sem("folded_all")
        bottomt_moved = sem("bottomt_moved")
        ident_zero = sem("ident_zero")
        ident_ready = sem("ident_ready")
        pads_zero = sem("pads_zero")
        w1_in = sem("w1_in")
        w2_in = sem("w2_in")
        vecs_in = sem("vecs_in")
        xt_full = [sem(f"xt_full{k}") for k in range(2)]
        xt_moved = [sem(f"xt_moved{k}") for k in range(2)]
        gram_full = sem("gram_full")
        gram_dve = sem("gram_dve")
        gram_act = sem("gram_act")
        z_ready = sem("z_ready")
        zt_full = sem("zt_full")
        zt_moved = sem("zt_moved")
        h1_full = sem("h1_full")
        h1_moved = sem("h1_moved")
        h2_full = sem("h2_full")
        h2_moved = sem("h2_moved")
        prod_done = sem("prod_done")
        y_ready = sem("y_ready")
        y_out = sem("y_out")
        all_ids_in = sem("all_ids_in")
        ids_hot_ready = sem("ids_hot_ready")
        idents_cast = sem("idents_cast")
        rows_counted = sem("rows_counted")
        rows_wide = sem("rows_wide")
        tab_in = [sem(f"tab_in{u}") for u in range(HOT)]
        tab_cast = [sem(f"tab_cast{k}") for k in range(2)]
        tab_rest = sem("tab_rest")
        tab_last = sem("tab_last")
        wide_full = sem("wide_full")
        wide_moved = sem("wide_moved")
        onehot_ready = sem("onehot_ready")
        hot_full = sem("hot_full")
        hot_moved = sem("hot_moved")
        hot_steps = sem("hot_steps")
        hot_placed = sem("hot_placed")
        load_steps = sem("load_steps")
        gather_steps = sem("gather_steps")
        fold_steps = sem("fold_steps")

        block = ctx.enter_context(nc.Block())

        def slots_of(r):
            return [k for run in rounds[r] for k in run]

        def tables_of(r):
            return [k - 1 for k in slots_of(r) if k > 0]

        moves = [sum(len(rounds[r]) for r in range(k, ROUNDS, 2)) for k in range(2)]

        hot_moves, u0 = [], 0
        for rnd in hot_slots:
            for run in rnd:
                hot_moves.append((u0, run))
                u0 += len(run)

        def moves_before(r):
            return sum(len(rounds[q]) for q in range(r % 2, r, 2))

        def wait(eng, s, value):
            if not (isinstance(value, int) and value <= 0):
                eng.wait_ge(s, value)

        def pipeline(eng, step):
            last = TILES // 2 - 1
            step(0, 0, 0, False, True)
            step(1, 0, 1, True, True)
            with eng.Fori(1, last) as n:
                step(2 * n, n, 0, True, True)
                step(2 * n + 1, n, 1, True, True)
            step(2 * last, last, 0, True, False)
            step(2 * last + 1, last, 1, True, False)

        SPREADS = HOT * TILES // 4
        hot_banks = [bank[:, 0:PAIR] for bank in [hot_ps] + h1_ps]

        def late_spreads(i):
            return range(HOT + (SPREADS - HOT) * i // (2 * GRAM_STEPS),
                         HOT + (SPREADS - HOT) * (i + 1) // (2 * GRAM_STEPS))

        def spread_bank(k):
            return gram_ps[:, k % 2, :] if k < HOT else h1_ps[k % 2][:]

        def h1_part(c):
            return h1_ps[c // 2][:, P * (c % 2):P * (c % 2 + 1)]

        def bank_of(m, u):
            return hot_banks[u % len(hot_banks) if isinstance(m, int) and m == 0 else 0]

        def buffer_of(m, u):
            return onehot[(first_buffer if isinstance(m, int) and m == 0 else hot_buffer)[u]]

        def late_lookup(t, s):
            return s == 0 and not (isinstance(t, int) and t == 0)

        @block.sync
        def _(sp):
            def load_tile(t, s):
                wait(sp, xt_full[1], per_bank[1] * (t - 1))
                sp.sem_inc(load_steps, 1)
                sp.dma_start(idx[s][:], ids_v[:, t, :]).then_inc(ids_in[s], 16)
                sp.dma_start(X[s][:, 0, :], bottom_v[:, t, :]).then_inc(bottom_in[s], 16)

            load_tile(0, 0)
            sp.dma_start(ids_all[:], ids_v).then_inc(all_ids_in, 16)
            for u, f in enumerate(hot):
                sp.dma_start(tab[u], tables[f].rearrange("(p c) d -> p (c d)", p=HP)).then_inc(tab_in[u], 16)
            load_tile(1, 1)
            for c, row, count, w_row in w1_pieces():
                sp.dma_start(w1_sb[row:row + count, c, :], w1[w_row:w_row + count, :]).then_inc(w1_in, 16)
            sp.dma_start(w1_sb[:, len(CHUNKS), :], w1[PAIRS:PAIRS + D, :]).then_inc(w1_in, 16)
            sp.dma_start(w2_sb[:], w2.rearrange("(c p) n -> p c n", c=C1)).then_inc(w2_in, 16)
            for c in range(C1):
                sp.dma_start(b1_sb[:, c:c + 1], b1[P * c:P * (c + 1)].rearrange("(p o) -> p o", o=1)
                             ).then_inc(vecs_in, 16)
            sp.dma_start(b2_sb[:], b2.rearrange("(o n) -> o n", o=1).to_broadcast([P, N2])).then_inc(vecs_in, 16)
            sp.dma_start(w3_sb[:], w3.rearrange("n o -> o n").to_broadcast([P, N2])).then_inc(vecs_in, 16)
            with sp.Fori(1, TILES // 2) as n:
                load_tile(2 * n, 0)
                load_tile(2 * n + 1, 1)
            sp.wait_ge(y_ready, TILES)
            sp.dma_start(out.rearrange("(p t) o -> p (t o)", t=TILES), y[:]).then_inc(y_out, 16)
            sp.wait_ge(y_out, 16)

        w1_loads = 1 + len(w1_pieces())

        @block.gpsimd
        def _(pool):
            def gather(t, n, s):
                pool.wait_ge(ids_in[s], 16 * (n + 1))
                wait(pool, xt_full[1], per_bank[1] * (t - 1))
                pool.sem_inc(gather_steps, 1)
                for r in range(ROUNDS):
                    for f in tables_of(r):
                        column = first_column[r] + slots_of(r).index(1 + f)
                        pool.indirect_dma_start(X[s][:, column, :], None, tables[f],
                                                bass.IndirectOffsetOnAxis(idx[s][:, f:f + 1], 0)
                                                ).then_inc(gathered[s][r], 16)

            pool.memset(ident[:], 0.0).then_inc(ident_zero, 1)
            pool.wait_ge(ident_zero, 1)
            pool.affine_select(out=ident[:], in_=ident[:], compare_op=ALU.not_equal, fill=1.0, base=0,
                               pattern=[[-1, P]], channel_multiplier=1).then_inc(ident_ready, 1)
            pool.memset(fill_mask[:], 1.0).then_inc(mask_ones, 1)
            pool.wait_ge(mask_ones, 1)
            pool.affine_select(out=fill_mask[:], in_=fill_mask[:], compare_op=ALU.is_ge, fill=0.0,
                               base=HALF - 2, pattern=[[-1, HALF - 1], [-1, HALF - 1]], channel_multiplier=0
                               ).then_inc(mask_ready, 1)
            pool.iota(row_number[:], pattern=[[1, HC]], base=0, channel_multiplier=HC,
                      allow_small_or_imprecise_dtypes=True).then_inc(rows_counted, 1)
            gather(0, 0, 0)
            gather(1, 0, 1)
            with pool.Fori(1, TILES // 2) as n:
                gather(2 * n, n, 0)
                gather(2 * n + 1, n, 1)

        @block.tensor
        def _(pe):
            def spread_ids(steps):
                for k in steps:
                    u, four = k % HOT, k // HOT
                    wait(pe, wide_moved, k - 1)
                    for j in range(4):
                        t = 4 * four + j
                        mm = pe.matmul(spread_bank(k)[:, P * j:P * (j + 1)],
                                       ids_hot[:, u, t:t + 1].to_broadcast([P, P]), ident_fp16[:],
                                       start=True, stop=True)
                    mm.then_inc(wide_full, 1)

            def lookup(m, u, part_from, part_to):
                if part_from == 0:
                    pe.wait_ge(onehot_ready, HOT * m + u + 1)
                    wait(pe, hot_moved, u + 1 - len(hot_banks) if isinstance(m, int) and m == 0 else HOT * m + u)
                for k in range(part_from, part_to):
                    part, c = k // HC, k % HC
                    mm = pe.matmul(bank_of(m, u), tab_parts[:, u, part, D * c:D * (c + 1)],
                                   buffer_of(m, u)[:, c, :], start=(k == 0), stop=(k == PARTS * HC - 1))
                if part_to == PARTS * HC:
                    mm.then_inc(hot_full, 1)

            def lookup_segment(m, j):
                half = PARTS * HC // 2
                lookup(m, j // 2, half * (j % 2), half * (j % 2 + 1))

            def transposes(t, n, s, r):
                k = r % 2
                if r == 0:
                    pe.wait_ge(bottom_in[s], 16 * (n + 1))
                pe.wait_ge(gathered[s][r], 16 * len(tables_of(r)) * (n + 1))
                wait(pe, xt_moved[k], moves[k] * t + moves_before(r))
                for j in range(len(slots_of(r))):
                    halves = X[s][:, first_column[r] + j, :].bitcast(bf16).rearrange("p (d h) -> p h d", h=2)
                    for h in range(2):
                        mm = pe.transpose(xt_ps[k][:, 2 * j + h, :], halves[:, h, :], ident_bf[:])
                mm.then_inc(xt_full[k], 1)

            def gram(t, s, r):
                if r == 0:
                    pe.wait_ge(xt_moved[0], moves[0] * (t + 1))
                    pe.wait_ge(xt_moved[1], moves[1] * (t + 1))
                    pe.wait_ge(hot_placed, len(hot_moves) * (t + 1))
                for b in range(2):
                    half = 2 * GRAM_STEPS * t + 2 * r + b
                    wait(pe, gram_dve, half - 1)
                    wait(pe, gram_act, half - 1)
                    for k in range(GROUPS_PER_STEP // 2):
                        grp = GROUPS_PER_STEP * r + GROUPS_PER_STEP // 2 * b + k
                        four = XT[s][:, 4 * grp:4 * (grp + 1), :]
                        mm = pe.matmul(gram_ps[0:ROWS, b, k * 4 * NG:(k + 1) * 4 * NG],
                                       four.rearrange("d q f -> d (q f)")[:, 0:ROWS], four[:, :, 1:SLOTS],
                                       start=True, stop=True)
                    mm.then_inc(gram_full, 1)

            def z_transposes(t):
                pe.wait_ge(folded_all, t + 1)
                wait(pe, h2_moved, t)
                pairs = folded[:].rearrange("p r c -> p (r c)")[:, HALF:HALF + PAIRS]
                for c, k in enumerate(CHUNKS):
                    mm = pe.transpose(zt_ps[0:k, c, :], pairs[:, P * c:P * c + k], ident[:])
                mm.then_inc(zt_full, 1)

            def bottom_part(s, c):
                pe.matmul(h1_part(c), w1_sb[:, len(CHUNKS), P * c:P * (c + 1)], bottomT[s][:], start=True, stop=False)

            def layer1_start(t, s):
                pe.wait_ge(w1_in, 16 * w1_loads)
                pe.wait_ge(bottomt_moved, t + 1)
                wait(pe, h1_moved, C1 * t)
                for c in range(0, C1, 2):
                    bottom_part(s, c)

            def layer1(t, s, c_from, c_to):
                if c_from == 0:
                    pe.wait_ge(zt_moved, t + 1)
                for c in range(c_from, c_to):
                    if c % 2 == 1:
                        bottom_part(s, c)
                    for j, k in enumerate(CHUNKS):
                        mm = pe.matmul(h1_part(c), w1_sb[0:k, j, P * c:P * (c + 1)], ZT[0:k, j, :],
                                       start=False, stop=(j == len(CHUNKS) - 1))
                    mm.then_inc(h1_full, 1)

            def layer2(t):
                pe.wait_ge(w2_in, 16)
                for c in range(C1):
                    pe.wait_ge(h1_moved, C1 * t + c + 1)
                    mm = pe.matmul(h2_ps[:, 0:N2], h1T[:, c, :], w2_sb[:, c, :], start=(c == 0), stop=(c == C1 - 1))
                mm.then_inc(h2_full, 1)

            def step(t, n, s, mlp, lookups):
                segments = iter(range(4) if s == 0 else range(4, 2 * HOT - 1))
                last = s == 1 and not lookups

                def segment():
                    if lookups:
                        lookup_segment(n + 1, next(segments))

                first = isinstance(t, int) and t == 0
                if not first:
                    transposes(t, n, s, 0)
                    transposes(t, n, s, 1)
                if late_lookup(t, s):
                    lookup_segment(n, 2 * HOT - 1)
                if s == 1:
                    segment()
                if last:
                    transposes(t, n, s, 2)
                    z_transposes(t - 1)
                    layer1_start(t - 1, 1 - s)
                    layer1(t - 1, 1 - s, 0, C1)
                    transposes(t, n, s, 3)
                    layer2(t - 1)
                    transposes(t, n, s, 4)
                    transposes(t, n, s, 5)
                else:
                    if mlp:
                        z_transposes(t - 1)
                    if not first:
                        transposes(t, n, s, 2)
                        transposes(t, n, s, 3)
                    if mlp:
                        layer1_start(t - 1, 1 - s)
                        layer1(t - 1, 1 - s, 0, C1 // 2)
                    if not first:
                        transposes(t, n, s, 4)
                        transposes(t, n, s, 5)
                    if mlp:
                        layer1(t - 1, 1 - s, C1 // 2, C1)
                for r in range(GRAM_STEPS):
                    if r != 1:
                        segment()
                    elif mlp and not last:
                        layer2(t - 1)
                    if first:
                        spread_ids(late_spreads(2 * r))
                    gram(t, s, r)
                    if first:
                        spread_ids(late_spreads(2 * r + 1))
                segment()

            assert ROUNDS == 6 and GRAM_STEPS == 4 and HOT == 5
            pe.wait_ge(idents_cast, 2)
            pe.wait_ge(ids_hot_ready, HOT)
            pe.wait_ge(pads_zero, 3)
            spread_ids(range(HOT))
            for u in range(HOT):
                if u == 0:
                    transposes(0, 0, 0, 0)
                    transposes(0, 0, 0, 1)
                if u >= HOT - 2:
                    transposes(0, 0, 0, 2 * (u - HOT + 3))
                    transposes(0, 0, 0, 2 * (u - HOT + 3) + 1)
                pe.wait_ge(tab_cast[0], u + 1)
                pe.wait_ge(tab_cast[1], u + 1)
                pe.wait_ge(tab_last, u + 1)
                lookup(0, u, 0, PARTS * HC)
            pe.wait_ge(hot_moved, HOT)
            pipeline(pe, step)
            layer1_start(TILES - 1, 1)
            z_transposes(TILES - 1)
            layer1(TILES - 1, 1, 0, C1)
            layer2(TILES - 1)

        def move_xt(eng, copy, t, n, s, r):
            k = r % 2
            eng.wait_ge(xt_full[k], per_bank[k] * t + r // 2 + 1)
            wait(eng, gram_full, 2 * GRAM_STEPS * (t - 1))
            j = 0
            for run in rounds[r]:
                m = len(run)
                dst = XT16[s][:, :, 2 * run[0]:2 * (run[0] + m)].rearrange("d (grp q) c -> d c q grp", q=4)
                src = xt_ps[k][:, 2 * j:2 * (j + m), :].bitcast(i16).rearrange("d c (q grp) -> d c q grp", q=4)
                copy(dst, src).then_inc(xt_moved[k], 1)
                j += m

        def move_gram(eng, copy, t, r, quadrants, done, fine):
            for first, banks in ((0, 1), (1, 1)) if fine else ((0, 2),):
                eng.wait_ge(gram_full, 2 * GRAM_STEPS * t + 2 * r + first + banks)
                wait(eng, z_ready, t)
                for q in quadrants:
                    rows = slice(PAD * q, PAD * (q + 1))
                    src = gram_ps[rows, first:first + banks, 0:16 * NG].rearrange("p b (m n) -> p b m n", n=4 * NG)
                    group = GROUPS_PER_STEP * r + GROUPS_PER_STEP // 2 * first
                    dst = gram_sb[rows, :, group:group + GROUPS_PER_STEP // 2 * banks]
                    last = copy(dst.rearrange("p g (b m) -> p b m g", b=banks), src[:, :, :, NG * q:NG * (q + 1)])
                last.then_inc(done, banks)

        @block.vector
        def _(dve):
            copy = nc.vector.tensor_copy

            def z_blocks(t):
                dve.wait_ge(gram_dve, 2 * GRAM_STEPS * (t + 1))
                dve.wait_ge(gram_act, 2 * GRAM_STEPS * (t + 1))
                wait(dve, folded_all, t)
                dve.transpose(Z[:].rearrange("p g f -> p (g f)"),
                              gram_sb[:].rearrange("p g r -> p (g r)")).then_inc(z_ready, 1)
                dve.wait_ge(z_ready, t + 1)
                wait(dve, zt_full, t)
                dve.tensor_copy(folded[:], Z[:, :, HALF::-1].rearrange("p g f -> p f g")).then_inc(folded_high, 1)
                dve.wait_ge(folded_high, t + 1)
                dve.sem_inc(fold_steps, 1)
                first = PAD * (HALF - 1) + HALF + 1 + PAD + 1
                low = Z[:].rearrange("p g f -> p (g f)")[:, first:first + (PAD + 1) * (HALF - 1)]
                dve.copy_predicated(folded[:, 1:HALF, 0:HALF - 1], fill_mask[:].bitcast(mybir.dt.int32),
                                    low.rearrange("p (r c) -> p r c", c=PAD + 1)[:, :, 0:HALF - 1]
                                    ).then_inc(folded_all, 1)

            def one_hot(m, u):
                dve.wait_ge(wide_moved, SPREADS if not isinstance(m, int) else HOT if m == 1 else u + 1)
                if isinstance(m, int) and m == 0:
                    wait(dve, hot_full, u + 1 - hot_buffers)
                elif u == 0 and isinstance(m, int) and m == 1:
                    dve.wait_ge(hot_full, HOT)
                else:
                    before = [v for v in range(u) if hot_buffer[v] == hot_buffer[u]]
                    if before:
                        dve.wait_ge(hot_full, HOT * m + before[-1] + 1)
                    else:
                        last = max(v for v in range(HOT) if hot_buffer[v] == hot_buffer[u])
                        wait(dve, hot_full, HOT * (m - 1) + last + 1)
                ids_of = ids_wide[0:HP, u:u + 1, bass.ds(PAIR * m, PAIR)]
                dve.tensor_tensor(buffer_of(m, u)[:], ids_of.to_broadcast([HP, HC, PAIR]),
                                  row_wide[0:HP], ALU.is_equal).then_inc(onehot_ready, 1)

            def move_zt(t):
                dve.wait_ge(zt_full, t + 1)
                wait(dve, h1_full, C1 * t)
                dve.tensor_copy(ZT[:], zt_ps[:]).then_inc(zt_moved, 1)

            def layer3(t):
                dve.wait_ge(h2_full, t + 1)
                wait(dve, prod_done, t)
                dve.tensor_tensor(h2[:], h2_ps[:, 0:N2], b2_sb[:], ALU.add).then_inc(h2_moved, 1)
                dve.wait_ge(h2_moved, t + 1)
                wait(dve, y_ready, t)
                dve.scalar_tensor_tensor(prod[:], h2[:], 0.0, w3_sb[:], ALU.max, ALU.mult,
                                         accum_out=ysum[:]).then_inc(prod_done, 1)
                dve.wait_ge(prod_done, t + 1)
                dve.tensor_copy(y[:, bass.ds(t, 1)], ysum[:]).then_inc(y_ready, 1)

            def step(t, n, s, mlp, lookups):
                if lookups and s == 0:
                    one_hot(n + 1, 0)
                last = s == 1 and not lookups
                if mlp:
                    move_zt(t - 1)
                if not (isinstance(t, int) and t == 0):
                    move_xt(dve, copy, t, n, s, 2)
                    move_xt(dve, copy, t, n, s, 4)
                if lookups:
                    one_hot(n + 1, (1, 3)[s])
                if last:
                    layer3(t - 1)
                move_gram(dve, copy, t, 0, (0, 1), gram_dve, not lookups)
                if mlp and not last:
                    layer3(t - 1)
                move_gram(dve, copy, t, 1, (0, 1), gram_dve, not lookups)
                if lookups and s == 1:
                    one_hot(n + 1, 4)
                move_gram(dve, copy, t, 2, (0, 1), gram_dve, not lookups)
                if lookups and s == 0:
                    one_hot(n + 1, 2)
                move_gram(dve, copy, t, 3, (0, 1), gram_dve, not lookups)
                z_blocks(t)

            for s in range(2):
                dve.memset(XT[s][:, :, SLOTS:PAD], 0.0).then_inc(pads_zero, 1)
            dve.memset(zt_ps[:], 0.0).then_inc(pads_zero, 1)
            dve.wait_ge(ident_ready, 1)
            dve.tensor_copy(ident_fp16[:], ident[:]).then_inc(idents_cast, 1)
            dve.tensor_copy(ident_bf[:], ident[:]).then_inc(idents_cast, 1)
            dve.wait_ge(rows_counted, 1)
            dve.tensor_copy(row_wide[:], row_number[:].rearrange("p (c o) -> p c o", o=1
                                                                 ).to_broadcast([P, HC, PAIR])).then_inc(rows_wide, 1)
            dve.wait_ge(all_ids_in, 16)
            for u, f in enumerate(hot):
                dve.tensor_copy(ids_hot[:, u, :], ids_all[:, :, f]).then_inc(ids_hot_ready, 1)
            dve.wait_ge(rows_wide, 1)

            def after_part0(u):
                dve.wait_ge(tab_cast[0], u + 1)
                dve.tensor_tensor(tab[u], tab[u], tab_parts[:, u, 0, :], ALU.subtract).then_inc(tab_rest, 1)

            after_part0(0)
            for u in range(HOT):
                if u + 1 < HOT:
                    after_part0(u + 1)
                dve.wait_ge(tab_cast[1], u + 1)
                dve.tensor_tensor(tab_parts[:, u, 2, :], tab[u], tab_parts[:, u, 1, :],
                                  ALU.subtract).then_inc(tab_last, 1)
                if u < hot_buffers:
                    one_hot(0, u)
            for u in range(hot_buffers, HOT):
                one_hot(0, u)
            move_xt(dve, copy, 0, 0, 0, 2)
            move_xt(dve, copy, 0, 0, 0, 4)
            dve.wait_ge(mask_ready, 1)
            dve.wait_ge(vecs_in, 16 * (C1 + 2))
            pipeline(dve, step)
            move_zt(TILES - 1)
            layer3(TILES - 1)

        @block.scalar
        def _(act):
            copy = nc.scalar.copy

            def move_bottom(t, s):
                act.wait_ge(xt_moved[0], moves[0] * t + 1)
                wait(act, h1_full, C1 * (t - 1))
                act.copy(bottomT[s][:].rearrange("d (q grp) -> d q grp", q=4),
                         XT[s][:, :, 0].rearrange("d (grp q) -> d q grp", q=4)).then_inc(bottomt_moved, 1)

            def relu_h1(t, c_from, c_to):
                for c in range(c_from, c_to):
                    act.wait_ge(h1_full, C1 * t + c // 2 * 2 + 2)
                    wait(act, h2_full, t)
                    act.activation(h1T[:, c, :], h1_part(c), ACT.Relu,
                                   bias=b1_sb[:, c:c + 1]).then_inc(h1_moved, 1)

            def keep_hot(m, u):
                act.wait_ge(hot_full, HOT * m + u + 1)
                act.sem_inc(hot_steps, 1)
                act.copy(hotT[:, u, bass.ds(PAIR * m, PAIR)], bank_of(m, u)).then_inc(hot_moved, 1)

            def place_hot(t, n, s):
                act.wait_ge(hot_moved, HOT * (n + 1))
                wait(act, gram_full, 2 * GRAM_STEPS * (t - 1))
                act.sem_inc(hot_steps, 1)
                for u0, run in hot_moves:
                    dst = XT[s][:, :, run[0]:run[0] + len(run)].rearrange("d (grp q) c -> d c q grp", q=4)
                    src = hotT[:, u0:u0 + len(run), bass.ds(P * t, P)].rearrange("d c (q grp) -> d c q grp", q=4)
                    act.copy(dst, src).then_inc(hot_placed, 1)

            def keep_spreads(t, i):
                if isinstance(t, int) and t == 0:
                    for k in late_spreads(i):
                        keep_spread(k)

            def step(t, n, s, mlp, lookups):
                first = isinstance(t, int) and t == 0
                if not first:
                    move_xt(act, copy, t, n, s, 0)
                    move_xt(act, copy, t, n, s, 1)
                if late_lookup(t, s):
                    keep_hot(n, HOT - 1)
                last = s == 1 and not lookups
                if last:
                    place_hot(t, n, s)
                    relu_h1(t - 1, 0, C1)
                if not first:
                    move_xt(act, copy, t, n, s, 3)
                if not last:
                    place_hot(t, n, s)
                if mlp and not last:
                    relu_h1(t - 1, 0, C1 // 2)
                if not first:
                    move_xt(act, copy, t, n, s, 5)
                move_bottom(t, s)
                if mlp and not last:
                    relu_h1(t - 1, C1 // 2, C1)
                if lookups and s == 1:
                    keep_hot(n + 1, 2)
                keep_spreads(t, 0)
                move_gram(act, copy, t, 0, (2, 3), gram_act, not lookups)
                keep_spreads(t, 1)
                keep_spreads(t, 2)
                move_gram(act, copy, t, 1, (2, 3), gram_act, not lookups)
                keep_spreads(t, 3)
                if lookups and s == 0:
                    keep_hot(n + 1, 0)
                keep_spreads(t, 4)
                move_gram(act, copy, t, 2, (2, 3), gram_act, not lookups)
                keep_spreads(t, 5)
                if lookups and s == 1:
                    keep_hot(n + 1, 3)
                keep_spreads(t, 6)
                move_gram(act, copy, t, 3, (2, 3), gram_act, not lookups)
                keep_spreads(t, 7)
                if lookups and s == 0:
                    keep_hot(n + 1, 1)

            def part0(u):
                act.wait_ge(tab_in[u], 16)
                act.copy(tab_parts[:, u, 0, :], tab[u]).then_inc(tab_cast[0], 1)

            def keep_spread(k):
                act.wait_ge(wide_full, k + 1)
                u, four = k % HOT, k // HOT
                act.copy(ids_wide[:, u, 4 * P * four:4 * P * (four + 1)], spread_bank(k)
                         ).then_inc(wide_moved, 1)

            part0(0)
            part0(1)
            keep_spread(0)
            for u in range(HOT):
                act.wait_ge(tab_rest, u + 1)
                act.copy(tab_parts[:, u, 1, :], tab[u]).then_inc(tab_cast[1], 1)
                if u + 2 < HOT:
                    part0(u + 2)
                if u + 1 < HOT:
                    keep_spread(u + 1)
            for u in range(HOT):
                keep_hot(0, u)
                if u < 2:
                    move_xt(act, copy, 0, 0, 0, u)
                if u >= HOT - 3 and u < HOT - 1:
                    move_xt(act, copy, 0, 0, 0, 2 * (u - HOT + 3) + 3)
            act.wait_ge(vecs_in, 16 * (C1 + 2))
            pipeline(act, step)
            relu_h1(TILES - 1, 0, C1)


_INS = (["r_bottom_output", "ids"] + [f"tbl_{f}" for f in range(TABLES)]
        + ["W_top1", "b_top1", "W_top2", "b_top2", "W_top3"])


def kernel(**inputs):
    import numpy as _np
    import concourse.bacc as _bacc
    from concourse import mybir as _mybir
    from concourse.bass_utils import run_bass_kernel_spmd as _run

    nc = _bacc.Bacc("TRN2", target_bir_lowering=False, num_devices=1)
    arrays, dram = {}, {}
    for name in _INS:
        a = _np.ascontiguousarray(inputs[name])
        arrays[f"in_{name}_dram"] = a
        dram[name] = nc.dram_tensor(f"in_{name}_dram", a.shape, _mybir.dt.from_np(a.dtype),
                                    kind="ExternalInput").ap()
    out = nc.dram_tensor("out_0_dram", (BATCH, 1), _mybir.dt.float32, kind="ExternalOutput").ap()
    build(nc, dram["r_bottom_output"], dram["ids"], [dram[f"tbl_{f}"] for f in range(TABLES)],
          dram["W_top1"], dram["b_top1"], dram["W_top2"], dram["b_top2"], dram["W_top3"], out)
    r = _run(nc, [arrays], core_ids=[0])
    return r.results[0]["out_0_dram"]
```
